# Optimizing a Trainium2 kernel written in Bass

```python
import numpy as np
import jax
import jax.numpy as jnp

def _softmax(x, axis=-1):
    return jax.nn.softmax(x, axis=axis)

def _gelu(x):
    return jax.nn.gelu(x, approximate=True)

def _silu(x):
    return jax.nn.silu(x)

def _sigmoid(x):
    return jax.nn.sigmoid(x)

def _layernorm(x, axis=-1, eps=1e-05):
    m = jnp.mean(x, axis=axis, keepdims=True)
    v = jnp.var(x, axis=axis, keepdims=True)
    return (x - m) / jnp.sqrt(v + eps)

def _scatter_add(tgt, idx, src, axis=0):
    return tgt.at[idx].add(src)

def _segment_sum(src, seg, n):
    return jax.ops.segment_sum(src, seg, n)
kernel_name = 'mk_adj_resnorm_d1_adj_r2_177c25'

def setup_inputs(seed: int=0):
    np.random.seed(seed)
    _w = jnp.asarray

    def _rec_inputs():
        import jax
        import jax.numpy as jnp
        _gk = jax.random.key(seed)
        x = -0.0002928 + 1 * jax.random.normal(jax.random.fold_in(_gk, 1), (4096, 256), jnp.float32)
        _a = jax.random.bernoulli(jax.random.fold_in(_gk, 2), 0.000976562, (4096, 4096))
        _a = jnp.logical_or(_a, jnp.eye(4096, dtype=bool))
        _af = _a.astype(jnp.float32)
        adj = _af
        return (x, adj)
    x, adj = _rec_inputs()

    def _L0_gnn_setup():
        import jax, jax.numpy as jnp
        import numpy as np
        N = 4096
        F_IN = 256
        F_OUT = 256
        DENSITY = 0.01
        key = jax.random.key(seed)
        k_x, k_adj, k_w, k_b = jax.random.split(key, 4)
        input_features = jax.random.normal(k_x, (N, F_IN), dtype=jnp.float32)
        adj = (jax.random.uniform(k_adj, (N, N)) < DENSITY).astype(jnp.float32)
        idx = jnp.arange(N)
        adj = adj.at[idx, idx].set(1.0)
        W = jax.random.normal(k_w, (F_IN, F_OUT), dtype=jnp.float32) / np.sqrt(F_IN)
        b = jax.random.normal(k_b, (F_OUT,), dtype=jnp.float32) * 0.01
        return {'input_features': input_features, 'adj': adj, 'W': W, 'b': b}
    _L0_gnn_all = _L0_gnn_setup()
    _L0_gnn_in = {k: v for k, v in _L0_gnn_all.items() if k in ('W', 'b')}
    del _L0_gnn_all
    return {'x': x, 'adj': adj, 'L0_gnn_W': _L0_gnn_in['W'], 'L0_gnn_b': _L0_gnn_in['b']}

def reference(x, adj, L0_gnn_W, L0_gnn_b):
    import jax
    import jax.numpy as jnp

    def _L0_gnn_ref(input_features, adj, W, b):
        import jax, jax.numpy as jnp
        import numpy as np
        N = 4096
        F_IN = 256
        F_OUT = 256
        DENSITY = 0.01
        A = (adj != 0).astype(input_features.dtype)
        hidden = input_features @ W + b
        deg = jnp.sum(A, axis=0)
        return A @ hidden / deg[:, None]
    x = _layernorm(x + _L0_gnn_ref(x, adj, L0_gnn_W, L0_gnn_b), axis=-1)
    return x

_drawn_inputs = setup_inputs


def setup_inputs(seed=0):
    import zlib

    import numpy as np

    out = dict(_drawn_inputs(seed))
    spreads = {}
    factors = {'L0_gnn_b': 5.607}
    for name, (base, spread) in spreads.items():
        noise = np.random.default_rng([zlib.crc32(name.encode()), seed]).standard_normal(out[name].shape)
        drawn = base * np.exp(spread * noise) if base else spread * noise
        out[name] = jnp.asarray(drawn.astype(out[name].dtype))
    for name, factor in factors.items():
        out[name] = (out[name] * factor).astype(out[name].dtype)
    return out
```

```python
from contextlib import ExitStack

import concourse.bass as bass
from concourse import mybir

P = 128
QUADS = 4
QP = P // QUADS
WORD = 4
MARK = 4
STAGE = 4
RING = 8
BANKS = 4
X_CHUNKS = 4
SPLIT = 4
EPS = 1e-5
MASK_AT = (10, 12, 14)

F32, F16, F8 = mybir.dt.float32, mybir.dt.float16, mybir.dt.float8e5
U8, U16, U32 = mybir.dt.uint8, mybir.dt.uint16, mybir.dt.uint32
ALU, ACT, AX = mybir.AluOpType, mybir.ActivationFunctionType, mybir.AxisListType


def build(nc, x, adj, w, b, out):
    N, F = x.shape
    T = N // P
    GROUPS = T // WORD
    QC = N // QUADS
    KC = F // P
    PAIRS = T // 2
    XG = GROUPS // X_CHUNKS
    PRELOAD = RING
    assert T % RING == 0 and RING % STAGE == 0 and RING % BANKS == 0 and F == 256 and T * MARK < 256
    assert QC == GROUPS * QP * WORD and STAGE == WORD

    x_v = x.rearrange("(q m a e) f -> q a m (e f)", q=QUADS, m=GROUPS, a=QP, e=WORD)
    out_v = out.rearrange("(q m a e) f -> m q a (e f)", q=QUADS, m=GROUPS, a=QP, e=WORD)
    adj_v = adj.rearrange("(r m a e) (q c) -> m e q a r c", r=QUADS, m=GROUPS, a=QP, e=WORD, q=QUADS)
    w_v = w.rearrange("(c p) f -> p c f", c=KC)

    with ExitStack() as ctx:
        def sb(name, shape, dt):
            return ctx.enter_context(nc.sbuf_tensor(name, shape, dt))

        def sem(name):
            return ctx.enter_context(nc.semaphore(name))

        x_sb = sb("x_sb", [P, T, F], F32)
        g_sb = sb("g_sb", [P, T, F], F32)
        parts = sb("parts", [P, T, 2 * F], F16)
        adj_f = sb("adj_f", [P, STAGE, QUADS, QC], F32)
        mask8 = sb("mask8", [P, QUADS, QC], U8)
        maskT = sb("maskT", [P, RING, GROUPS, P], U32)
        hilo = sb("hilo", [P, 2, 2 * F], F32)
        deg_acc = sb("deg_acc", [P, GROUPS, P], U32)
        stats = sb("stats", [P, WORD, 6], F32)
        mv = sb("mv", [P, 2, WORD, 2], F32)
        std = sb("std", [P, 2, WORD], F32)
        rstd = sb("rstd", [P, 2, WORD], F32)
        shift = sb("shift", [P, 2, WORD], F32)
        rdeg4 = sb("rdeg4", [P, T], F32)
        deg4 = sb("deg4", [P, T], F32)
        inv_deg = sb("inv_deg", [P, T], F32)
        pair_max = sb("pair_max", [P, PAIRS], F32)
        col = sb("col", [P, 8], F32)
        early = parts[:].rearrange("p t f -> p (t f)").bitcast(F32)
        w_sb = early[:, 0:KC * F].rearrange("p (c f) -> p c f", c=KC)
        b_sb = early[:, 512:512 + F]
        ident = early[:, 768:768 + P]
        ones = early[:, 896:896 + P]
        xT_sb = early[:, 1024:2048].rearrange("p (k j n) -> p k j n", k=2, j=2 * KC)
        y_sb = adj_f[:, 0].rearrange("p g c -> p (g c)")[:, 0:2 * WORD * F].rearrange(
            "p (k e f) -> p k e f", k=2, e=WORD)
        part_max, all_max, lead, scale, unscale, eps = (col[:, i:i + 1] for i in range(6))

        agg = ctx.enter_context(nc.psum_tensor("agg", [P, BANKS, 2 * F], F32))
        xT_ps = ctx.enter_context(nc.psum_tensor("xT_ps", [P, 2, 2 * KC, P], F32))
        h_ps = ctx.enter_context(nc.psum_tensor("h_ps", [P, 2, 2, F], F32))

        w_landed = sem("w_landed")
        x_landed = [sem(f"x_landed{c}") for c in range(X_CHUNKS)]
        adj_landed = [sem(f"adj_landed{s}") for s in range(STAGE)]
        ident_zero, ident_ready = sem("ident_zero"), sem("ident_ready")
        zeros_ready = sem("zeros_ready")
        xT_ready, xT_copied = sem("xT_ready"), sem("xT_copied")
        h_ready, h_biased, h_maxed = sem("h_ready"), sem("h_biased"), sem("h_maxed")
        max_step, max_turned, max_spread = sem("max_step"), sem("max_turned"), sem("max_spread")
        scale_ready = sem("scale_ready")
        hi_ready, lo_ready = sem("hi_ready"), sem("lo_ready")
        mask_made, maskT_ready, deg_added = sem("mask_made"), sem("maskT_ready"), sem("deg_added")
        agg_full, agg_copied, g_ready = sem("agg_full"), sem("agg_copied"), sem("g_ready")
        deg_step = sem("deg_step")
        y_ready, stats_ready, mv_ready = sem("y_ready"), sem("stats_ready"), sem("mv_ready")
        std_ready, rstd_ready, shift_ready = sem("std_ready"), sem("rstd_ready"), sem("shift_ready")
        out_ready, out_stored = sem("out_ready"), sem("out_stored")

        def load_adj(queue, m, e, quads):
            for q in quads:
                queue.dma_start(adj_f[q * QP:(q + 1) * QP, e], adj_v[m, e, q]).then_inc(adj_landed[e], 16)

        def load_x(queue, quads):
            for c in range(X_CHUNKS):
                for q in quads:
                    queue.dma_start(
                        x_sb[q * QP:(q + 1) * QP, c * XG * WORD:(c + 1) * XG * WORD, :],
                        x_v[q, :, c * XG:(c + 1) * XG]).then_inc(x_landed[c], 16)

        block = ctx.enter_context(nc.Block())

        @block.sync
        def _(sp):
            sp.dma_start(w_sb, w_v).then_inc(w_landed, 16)
            load_x(sp, (0, 1))
            for e in range(STAGE):
                load_adj(sp, 0, e, (0, 1))
            with sp.Fori(1, GROUPS) as m:
                for e in range(WORD):
                    sp.wait_ge(mask_made, WORD * m + (e - STAGE + 1))
                    load_adj(sp, m, e, (0, 1))
            with sp.Fori(0, GROUPS) as m:
                sp.wait_ge(out_ready, WORD * m + WORD)
                for q in range(QUADS):
                    sp.dma_start(out_v[m, q], g_sb[q * QP:(q + 1) * QP, bass.ts(m, WORD), :]).then_inc(out_stored, 16)
            sp.wait_ge(out_stored, 16 * QUADS * GROUPS)

        @block.gpsimd
        def _(pool):
            nc.gpsimd.memset(ident, 0.0).then_inc(ident_zero, 1)
            pool.wait_ge(ident_zero, 1)
            nc.gpsimd.affine_select(out=ident, in_=ident, compare_op=ALU.not_equal, fill=1.0, base=0,
                                    pattern=[[-1, P]], channel_multiplier=1).then_inc(ident_ready, 1)
            with pool.Fori(0, T // 2) as i:
                for j in range(2):
                    pool.wait_ge(agg_copied, 2 * i + (j + 1))
                    nc.gpsimd.tensor_tensor(g_sb[:, bass.ds(2 * i + j, 1), :], hilo[:, j:j + 1, 0:F], hilo[:, j:j + 1, F:2 * F],
                                            ALU.add).then_inc(g_ready, 1)

        @block.scalar
        def _(act):
            act.dma_start(b_sb, b.rearrange("(a f) -> a f", a=1).broadcast_to([P, F])).then_inc(w_landed, 16)
            load_x(act, (2, 3))
            for e in range(STAGE):
                load_adj(act, 0, e, (2, 3))

            with act.Fori(0, PAIRS // 2) as i:
                for j in range(2):
                    act.wait_ge(xT_ready, 2 * i + (j + 1))
                    act.wait_ge(h_ready, 2 * i + (j - 1)) if j == 1 else act.wait_ge(h_ready, 2 * i)
                    nc.scalar.copy(xT_sb[:, j], xT_ps[:, j]).then_inc(xT_copied, 1)

            for e in range(STAGE, STAGE + len(MASK_AT)):
                act.wait_ge(mask_made, e - STAGE + 1)
                load_adj(act, e // WORD, e % WORD, (2, 3))

            act.wait_ge(scale_ready, 1)
            for c in range(T // SPLIT):
                nc.scalar.activation(parts[:, SPLIT * c:SPLIT * (c + 1), 0:F], g_sb[:, SPLIT * c:SPLIT * (c + 1), :],
                                     ACT.Copy, scale=scale).then_inc(hi_ready, 1)

            for e in range(STAGE + len(MASK_AT), PRELOAD):
                act.wait_ge(mask_made, e - STAGE + 1)
                load_adj(act, e // WORD, e % WORD, (2, 3))

            def copy_aggregate(t, k):
                act.wait_ge(agg_full, t + 1)
                act.wait_ge(g_ready, t - 1)
                nc.scalar.copy(hilo[:, k % 2], agg[:, k]).then_inc(agg_copied, 1)

            def normalise(m):
                act.wait_ge(shift_ready, m + 1)
                for e in range(WORD):
                    nc.scalar.activation(g_sb[:, WORD * m + e, :], y_sb[:, m % 2, e, :], ACT.Identity,
                                         scale=rstd[:, m % 2, e:e + 1],
                                         bias=shift[:, m % 2, e:e + 1]).then_inc(out_ready, 1)

            def root(m):
                act.wait_ge(mv_ready, WORD * m + WORD)
                nc.scalar.activation(std[:, m % 2], mv[:, m % 2, :, 1], ACT.Sqrt, bias=eps).then_inc(std_ready, 1)

            for t in range(BANKS):
                act.wait_ge(agg_full, t + 1)
                if t >= 2:
                    act.wait_ge(g_ready, t - 1)
                nc.scalar.copy(hilo[:, t % 2], agg[:, t]).then_inc(agg_copied, 1)
                act.wait_ge(mask_made, t + PRELOAD - STAGE + 1)
                load_adj(act, (t + PRELOAD) // WORD, t % WORD, (2, 3))
            with act.Fori(1, GROUPS - PRELOAD // WORD) as m:
                for e in range(WORD):
                    copy_aggregate(WORD * m + e, e)
                    act.wait_ge(mask_made, WORD * m + (e + PRELOAD - STAGE + 1))
                    load_adj(act, m + PRELOAD // WORD, e, (2, 3))
            done = T - PRELOAD
            for m in range(GROUPS - 1):
                copy_aggregate(done + m, (done + m) % BANKS)
                root(m)
                if m >= 1:
                    normalise(m - 1)
            copy_aggregate(T - 1, (T - 1) % BANKS)
            normalise(GROUPS - 2)
            root(GROUPS - 1)
            normalise(GROUPS - 1)

        @block.vector
        def _(dve):
            nc.vector.memset(deg_acc[:], 0).then_inc(zeros_ready, 1)
            nc.vector.memset(ones, 1.0).then_inc(zeros_ready, 1)
            nc.vector.memset(eps, EPS).then_inc(zeros_ready, 1)
            dve.wait_ge(w_landed, 32)

            def mask_slab(t, r, turn, first):
                dve.wait_ge(adj_landed[r % STAGE], 16 * QUADS * (turn + 1))
                if not (first and r == 0):
                    dve.wait_ge(maskT_ready, t)
                nc.vector.tensor_scalar(mask8[:], adj_f[:, r % STAGE], 0.0, float(MARK), ALU.not_equal,
                                        ALU.mult).then_inc(mask_made, 1)
                dve.wait_ge(mask_made, t + 1)
                if not first:
                    dve.wait_ge(agg_full, t - (RING - 1))
                nc.vector.transpose(
                    maskT[:, r].rearrange("p m (g a) -> p g m a", g=QUADS),
                    mask8[:].bitcast(U32).rearrange("p g (m a) -> p g m a", m=GROUPS)).then_inc(maskT_ready, 1)
                dve.wait_ge(maskT_ready, t + 1)
                if first and r == 0:
                    dve.wait_ge(zeros_ready, 3)
                else:
                    dve.wait_ge(deg_added, t)
                nc.vector.tensor_tensor(deg_acc[:].bitcast(U16), deg_acc[:].bitcast(U16),
                                        maskT[:, r].bitcast(U16), ALU.add).then_inc(deg_added, 1)

            def hidden_pair(u, k):
                h = g_sb[:, bass.ts(u, 2), :]
                dve.wait_ge(h_ready, u + 1)
                nc.vector.tensor_tensor(h, h_ps[:, k], b_sb.rearrange("p (k f) -> p k f", k=1).broadcast_to([P, 2, F]),
                                        ALU.add).then_inc(h_biased, 1)
                dve.wait_ge(h_biased, u + 1)
                nc.vector.tensor_reduce(pair_max[:, bass.ds(u, 1)], h, AX.XY, ALU.max,
                                        apply_absolute_value=True).then_inc(h_maxed, 1)

            with dve.Fori(0, PAIRS // 4) as i:
                for k in range(2):
                    hidden_pair(2 * i + k, k)
            for u in range(PAIRS // 2, PAIRS):
                hidden_pair(u, u % 2)
                if u in MASK_AT:
                    r = MASK_AT.index(u)
                    mask_slab(r, r, r // STAGE, True)

            dve.wait_ge(h_maxed, PAIRS)
            nc.vector.tensor_reduce(part_max, pair_max[:], AX.X, ALU.max).then_inc(max_step, 1)
            dve.wait_ge(max_turned, 1)
            nc.vector.tensor_reduce(all_max[0:1], xT_ps[0:1, 0, 0, :], AX.X, ALU.max).then_inc(max_step, 1)
            dve.wait_ge(max_spread, 1)
            nc.vector.tensor_scalar(lead, xT_ps[:, 1, 0, 0:1], 2.0 ** -100, None, ALU.max).then_inc(max_step, 1)
            dve.wait_ge(max_step, 3)
            nc.vector.tensor_scalar(unscale.bitcast(U32), lead.bitcast(U32), 0x7F800000, None,
                                    ALU.bitwise_and).then_inc(max_step, 1)
            dve.wait_ge(max_step, 4)
            nc.vector.reciprocal(lead, unscale).then_inc(max_step, 1)
            dve.wait_ge(max_step, 5)
            nc.vector.tensor_scalar(scale, lead, 2.0 ** 14, None, ALU.mult).then_inc(scale_ready, 1)
            dve.wait_ge(scale_ready, 1)
            for c in range(T // SPLIT):
                tiles = slice(SPLIT * c, SPLIT * (c + 1))
                dve.wait_ge(hi_ready, c + 1)
                nc.vector.scalar_tensor_tensor(out=parts[:, tiles, F:2 * F], in0=g_sb[:, tiles, :], scalar=scale,
                                               in1=parts[:, tiles, 0:F], op0=ALU.mult,
                                               op1=ALU.subtract).then_inc(lo_ready, 1)

            for r in range(len(MASK_AT), RING):
                mask_slab(r, r, r // STAGE, True)
            with dve.Fori(1, T // RING) as i:
                for r in range(RING):
                    mask_slab(RING * i + r, r, (RING // STAGE) * i + r // STAGE, False)

            dve.wait_ge(deg_added, T)
            deg_bytes = deg_acc[:].bitcast(U8).rearrange("p m (i e) -> p m e i", e=WORD)
            nc.vector.tensor_reduce(deg4[:].rearrange("p (m e) -> p m e", e=WORD), deg_bytes,
                                    AX.X, ALU.add).then_inc(deg_step, 1)
            dve.wait_ge(deg_step, 1)
            nc.vector.reciprocal(rdeg4[:], deg4[:]).then_inc(deg_step, 1)
            dve.wait_ge(deg_step, 2)
            nc.vector.tensor_scalar(inv_deg[:], rdeg4[:], unscale, float(MARK), ALU.mult, ALU.mult).then_inc(deg_step, 1)
            dve.wait_ge(deg_step, 3)

            def row_stats(m, k):
                for e in range(WORD):
                    t = WORD * m + e
                    dve.wait_ge(g_ready, t + 1)
                    nc.vector.scalar_tensor_tensor(out=y_sb[:, k, e, :], in0=g_sb[:, bass.ds(t, 1), :],
                                                   scalar=inv_deg[:, bass.ds(t, 1)],
                                                   in1=x_sb[:, bass.ds(t, 1), :], op0=ALU.mult,
                                                   op1=ALU.add).then_inc(y_ready, 1)
                    dve.wait_ge(y_ready, t + 1)
                    nc.vector.bn_stats(stats[:, e, :], y_sb[:, k, e, :]).then_inc(stats_ready, 1)
                    dve.wait_ge(deg_step, 3)
                    dve.wait_ge(stats_ready, t + 1)
                    nc.vector.bn_aggr(mv[:, k, e, :], stats[:, e, :]).then_inc(mv_ready, 1)

            def row_factors(m, k):
                dve.wait_ge(std_ready, m + 1)
                nc.vector.reciprocal(rstd[:, k], std[:, k]).then_inc(rstd_ready, 1)
                dve.wait_ge(rstd_ready, m + 1)
                nc.vector.scalar_tensor_tensor(out=shift[:, k], in0=mv[:, k, :, 0], scalar=-1.0, in1=rstd[:, k],
                                               op0=ALU.mult, op1=ALU.mult).then_inc(shift_ready, 1)

            row_stats(0, 0)
            row_stats(1, 1)
            row_factors(0, 0)
            with dve.Fori(1, GROUPS // 2) as i:
                for k in range(2):
                    dve.wait_ge(out_ready, WORD * (2 * i + (k - 1)))
                    row_stats(2 * i + k, k)
                    row_factors(2 * i + (k - 1), 1 - k)
            row_factors(GROUPS - 1, 1)

        @block.tensor
        def _(pe):
            pe.wait_ge(ident_ready, 1)
            pe.wait_ge(w_landed, 32)
            for u in range(PAIRS + 1):
                if u < PAIRS:
                    if u % (PAIRS // X_CHUNKS) == 0:
                        pe.wait_ge(x_landed[u // (PAIRS // X_CHUNKS)], 16 * QUADS)
                    if u >= 2:
                        pe.wait_ge(xT_copied, u - 1)
                    for j in range(2 * KC):
                        last = nc.tensor.transpose(xT_ps[:, u % 2, j, :], x_sb[:, 2 * u + j // KC, (j % KC) * P:(j % KC + 1) * P], ident)
                    last.then_inc(xT_ready, 1)
                if u >= 1:
                    v = u - 1
                    pe.wait_ge(xT_copied, v + 1)
                    if v >= 2:
                        pe.wait_ge(h_biased, v - 1)
                    for k in range(2):
                        for c in range(KC):
                            last = nc.tensor.matmul(h_ps[:, v % 2, k, :], xT_sb[:, v % 2, KC * k + c, :], w_sb[:, c, :],
                                                    start=(c == 0), stop=(c == KC - 1))
                    last.then_inc(h_ready, 1)

            pe.wait_ge(max_step, 1)
            nc.tensor.transpose(xT_ps[0:1, 0, 0, :], part_max, ident).then_inc(max_turned, 1)
            pe.wait_ge(max_step, 2)
            pe.wait_ge(zeros_ready, 3)
            nc.tensor.matmul(xT_ps[:, 1, 0, 0:1], ones[0:1, :], all_max[0:1, :], start=True,
                             stop=True).then_inc(max_spread, 1)

            def aggregate(t, r, first):
                if not first:
                    pe.reg_add(slabs_turned, slabs_turned, 1)
                    pe.reg_add(slabs_copied, slabs_copied, 1)
                    pe.wait_ge(lo_ready, T // SPLIT)
                    pe.wait_ge(maskT_ready, slabs_turned)
                    pe.wait_ge(agg_copied, slabs_copied)
                else:
                    pe.wait_ge(maskT_ready, t + 1)
                    if r >= BANKS:
                        pe.wait_ge(agg_copied, t - (BANKS - 1))
                for k in range(T):
                    if first and r == 0 and k % SPLIT == 0:
                        pe.wait_ge(lo_ready, k // SPLIT + 1)
                    words = maskT[:, r, k // WORD, :].bitcast(F8)
                    last = nc.tensor.matmul(agg[:, r % BANKS, :], words[:, k % WORD::WORD], parts[:, k, :],
                                            start=(k == 0), stop=(k == T - 1))
                last.then_inc(agg_full, 1)

            for r in range(RING):
                aggregate(r, r, True)
            slabs_turned, slabs_copied = pe.alloc_register("slabs_turned"), pe.alloc_register("slabs_copied")
            pe.reg_mov(slabs_turned, RING)
            pe.reg_mov(slabs_copied, RING - BANKS)
            with pe.Fori(1, T // RING) as i:
                for r in range(RING):
                    aggregate(RING * i + r, r, False)


_INS = ["x", "adj", "L0_gnn_W", "L0_gnn_b"]
_OUTS = [((4096, 256), "float32")]


def kernel(**inputs):
    import numpy as _np
    import concourse.bacc as _bacc
    from concourse import mybir as _mybir
    from concourse.bass_utils import run_bass_kernel_spmd as _run

    nc = _bacc.Bacc("TRN2", target_bir_lowering=False, num_devices=1)
    arrays, args = {}, []
    for name in _INS:
        a = _np.ascontiguousarray(inputs[name])
        arrays[f"in_{name}_dram"] = a
        args.append(nc.dram_tensor(f"in_{name}_dram", a.shape, _mybir.dt.from_np(a.dtype), kind="ExternalInput").ap())
    for i, (shape, dtype) in enumerate(_OUTS):
        dt = _mybir.dt.from_np(_np.dtype(dtype))
        args.append(nc.dram_tensor(f"out_{i}_dram", shape, dt, kind="ExternalOutput").ap())
    build(nc, *args)
    r = _run(nc, [arrays], core_ids=[0])
    got = tuple(r.results[0][f"out_{i}_dram"] for i in range(len(_OUTS)))
    return got[0]
```

```python
from contextlib import ExitStack

import concourse.bass as bass
from concourse import mybir

P = 128
QUADS = 4
QP = P // QUADS
WORD = 4
MARK = 4
STAGE = 4
RING = 8
BANKS = 4
X_CHUNKS = (1, 3, 4)
TURN, SPREAD, SPLIT = 8, 9, 10
LOAD_AT = (1, 3, 5, 7)
EPS = 1e-5

F32, F16, F8 = mybir.dt.float32, mybir.dt.float16, mybir.dt.float8e5
U8, U16, U32 = mybir.dt.uint8, mybir.dt.uint16, mybir.dt.uint32
ALU, ACT, AX = mybir.AluOpType, mybir.ActivationFunctionType, mybir.AxisListType


def build(nc, x, adj, w, b, out):
    N, F = x.shape
    T = N // P
    GROUPS = T // WORD
    QC = N // QUADS
    KC = F // P
    PAIRS = T // 2
    X_FROM = [sum(X_CHUNKS[:c]) for c in range(len(X_CHUNKS) + 1)]
    PRELOAD = RING
    assert T % RING == 0 and RING % STAGE == 0 and RING % BANKS == 0 and F == 256 and T * MARK < 256
    assert QC == GROUPS * QP * WORD and STAGE == WORD

    split_after, k = [[] for _ in range(PAIRS + 1)], 0
    for u in range(SPLIT, PAIRS):
        while k <= u - 1 and len(split_after[u]) < 2:
            split_after[u].append(k)
            k += 1
    split_after[PAIRS] = list(range(k, PAIRS))

    x_v = x.rearrange("(q m a e) f -> q a m (e f)", q=QUADS, m=GROUPS, a=QP, e=WORD)
    out_v = out.rearrange("(q m a e) f -> m q a (e f)", q=QUADS, m=GROUPS, a=QP, e=WORD)
    adj_v = adj.rearrange("(r m a e) (q c) -> m e q a r c", r=QUADS, m=GROUPS, a=QP, e=WORD, q=QUADS)
    w_v = w.rearrange("(c p) f -> p c f", c=KC)

    with ExitStack() as ctx:
        def sb(name, shape, dt):
            return ctx.enter_context(nc.sbuf_tensor(name, shape, dt))

        def sem(name):
            return ctx.enter_context(nc.semaphore(name))

        agg = ctx.enter_context(nc.psum_tensor("agg", [P, BANKS, 2 * F], F32))
        xT_ps = ctx.enter_context(nc.psum_tensor("xT_ps", [P, 2, 2 * KC, P], F32))
        h_ps = ctx.enter_context(nc.psum_tensor("h_ps", [P, 2, 2, F], F32))

        x_sb = sb("x_sb", [P, T, F], F32)
        g_sb = sb("g_sb", [P, T, F], F32)
        parts = sb("parts", [P, T, 2 * F], F16)
        adj_f = sb("adj_f", [P, STAGE, QUADS, QC], F32)
        mask8 = sb("mask8", [P, QUADS, QC], U8)
        maskT = sb("maskT", [P, RING, GROUPS, P], U32)
        hilo = sb("hilo", [P, 2, 2 * F], F32)
        deg_acc = sb("deg_acc", [P, GROUPS, P], U32)
        stats = sb("stats", [P, WORD, 6], F32)
        mv = sb("mv", [P, 2, WORD, 2], F32)
        std = sb("std", [P, 2, WORD], F32)
        rstd = sb("rstd", [P, 2, WORD], F32)
        shift = sb("shift", [P, 2, WORD], F32)
        rdeg4 = sb("rdeg4", [P, T], F32)
        newton = sb("newton", [P, 2, WORD], F32)
        deg4 = sb("deg4", [P, T], F32)
        inv_deg = sb("inv_deg", [P, T], F32)
        x_max = sb("x_max", [P, GROUPS], F32)
        col = sb("col", [P, 12], F32)
        early = maskT[:, RING - 2:RING].rearrange("p r m n -> p (r m n)").bitcast(F32)
        w_sb = early[:, 0:KC * F].rearrange("p (c f) -> p c f", c=KC)
        b_sb = early[:, 512:512 + F]
        ident = early[:, 768:768 + P]
        ones = early[:, 896:896 + P]
        xT_sb = early[:, 1024:2048].rearrange("p (k j n) -> p k j n", k=2, j=2 * KC)
        part_max, all_max, both_max = col[:, 0:2], col[:, 2:4], col[:, 4:6]
        b_max, lead, scale, unscale, eps, warm = (col[:, i:i + 1] for i in range(6, 12))
        max_rows, max_cols = agg[0:1, 2, 0:2 * P].rearrange("p (k n) -> p k n", k=2), agg[:, 3, 0:2]

        w_landed = sem("w_landed")
        x_landed = [sem(f"x_landed{c}") for c in range(len(X_CHUNKS))]
        adj_landed = [sem(f"adj_landed{s}") for s in range(STAGE)]
        ident_zero, ident_ready = sem("ident_zero"), sem("ident_ready")
        zeros_ready = sem("zeros_ready")
        xT_ready, xT_copied = sem("xT_ready"), sem("xT_copied")
        h_ready, h_biased, x_maxed = sem("h_ready"), sem("h_biased"), sem("x_maxed")
        max_step, max_turned, max_spread = sem("max_step"), sem("max_turned"), sem("max_spread")
        scale_ready = sem("scale_ready")
        hi_ready, lo_ready = sem("hi_ready"), sem("lo_ready")
        mask_made, maskT_ready, deg_added = sem("mask_made"), sem("maskT_ready"), sem("deg_added")
        agg_full, agg_copied, g_ready = sem("agg_full"), sem("agg_copied"), sem("g_ready")
        deg_step = sem("deg_step")
        hi_added = sem("hi_added")
        y_ready, stats_ready, mv_ready = sem("y_ready"), sem("stats_ready"), sem("mv_ready")
        std_ready, newton_step, shift_ready = sem("std_ready"), sem("newton_step"), sem("shift_ready")
        out_ready, out_stored = sem("out_ready"), sem("out_stored")

        def load_adj(queue, m, e, quads):
            for q in quads:
                queue.dma_start(adj_f[q * QP:(q + 1) * QP, e], adj_v[m, e, q]).then_inc(adj_landed[e], 16)

        def load_x(queue, c, quads):
            for q in quads:
                queue.dma_start(x_sb[q * QP:(q + 1) * QP, X_FROM[c] * WORD:X_FROM[c + 1] * WORD, :],
                                x_v[q, :, X_FROM[c]:X_FROM[c + 1]]).then_inc(x_landed[c], 16)

        def x_chunk_of(group):
            return max(c for c in range(len(X_CHUNKS)) if X_FROM[c] <= group)

        block = ctx.enter_context(nc.Block())

        @block.sync
        def _(sp):
            load_x(sp, 0, (0, 1))
            sp.dma_start(w_sb, w_v).then_inc(w_landed, 16)
            for c in range(1, len(X_CHUNKS)):
                load_x(sp, c, (0, 1))
            for e in range(STAGE):
                load_adj(sp, 0, e, (0, 1))
            with sp.Fori(1, GROUPS) as m:
                for e in range(WORD):
                    sp.wait_ge(mask_made, WORD * m + (e - STAGE + 1))
                    load_adj(sp, m, e, (0, 1))
            with sp.Fori(0, GROUPS) as m:
                sp.wait_ge(out_ready, WORD * m + WORD)
                for q in range(QUADS):
                    sp.dma_start(out_v[m, q], g_sb[q * QP:(q + 1) * QP, bass.ts(m, WORD), :]).then_inc(out_stored, 16)
            sp.wait_ge(out_stored, 16 * QUADS * GROUPS)

        @block.gpsimd
        def _(pool):
            nc.gpsimd.memset(ident, 0.0).then_inc(ident_zero, 1)
            pool.wait_ge(ident_zero, 1)
            nc.gpsimd.affine_select(out=ident, in_=ident, compare_op=ALU.not_equal, fill=1.0, base=0,
                                    pattern=[[-1, P]], channel_multiplier=1).then_inc(ident_ready, 1)
            with pool.Fori(0, (T - WORD) // 2) as i:
                for j in range(2):
                    pool.wait_ge(agg_copied, 2 * i + (j + 1))
                    nc.gpsimd.tensor_tensor(g_sb[:, bass.ds(2 * i + j, 1), :], hilo[:, j:j + 1, 0:F], hilo[:, j:j + 1, F:2 * F],
                                            ALU.add).then_inc(g_ready, 1)

        @block.scalar
        def _(act):
            load_x(act, 0, (2, 3))
            act.wait_ge(zeros_ready, 1)
            nc.scalar.copy(warm, eps)
            act.dma_start(b_sb, b.rearrange("(a f) -> a f", a=1).broadcast_to([P, F])).then_inc(w_landed, 16)
            for c in range(1, len(X_CHUNKS)):
                load_x(act, c, (2, 3))

            def split_hi(u):
                act.wait_ge(h_biased, u + 1)
                nc.scalar.activation(parts[:, 2 * u:2 * u + 2, 0:F], g_sb[:, 2 * u:2 * u + 2, :],
                                     ACT.Copy, scale=scale).then_inc(hi_ready, 1)

            for u in range(PAIRS):
                act.wait_ge(xT_ready, u + 1)
                if u >= 2:
                    act.wait_ge(h_ready, u - 1)
                nc.scalar.copy(xT_sb[:, u % 2], xT_ps[:, u % 2]).then_inc(xT_copied, 1)
                if u in LOAD_AT:
                    load_adj(act, 0, LOAD_AT.index(u), (2, 3))
                if u == SPLIT + 1:
                    act.wait_ge(scale_ready, 1)
                for k in split_after[max(u - 1, 0)]:
                    split_hi(k)
            for k in split_after[PAIRS - 1] + split_after[PAIRS]:
                split_hi(k)
            for t in range(STAGE, PRELOAD):
                act.wait_ge(mask_made, t - STAGE + 1)
                load_adj(act, t // WORD, t % WORD, (2, 3))

            def copy_aggregate(t, k):
                act.wait_ge(agg_full, t + 1)
                act.wait_ge(g_ready, t - 1)
                nc.scalar.copy(hilo[:, k % 2], agg[:, k]).then_inc(agg_copied, 1)

            def normalise(m):
                act.wait_ge(shift_ready, m + 1)
                for e in range(WORD):
                    nc.scalar.activation(g_sb[:, WORD * m + e, :], g_sb[:, WORD * m + e, :], ACT.Identity,
                                         scale=rstd[:, m % 2, e:e + 1],
                                         bias=shift[:, m % 2, e:e + 1]).then_inc(out_ready, 1)

            def root(m):
                act.wait_ge(mv_ready, WORD * m + WORD)
                nc.scalar.activation(std[:, m % 2], mv[:, m % 2, :, 1], ACT.Sqrt, bias=eps).then_inc(std_ready, 1)

            for t in range(BANKS):
                act.wait_ge(agg_full, t + 1)
                if t >= 2:
                    act.wait_ge(g_ready, t - 1)
                nc.scalar.copy(hilo[:, t % 2], agg[:, t]).then_inc(agg_copied, 1)
                act.wait_ge(mask_made, t + PRELOAD - STAGE + 1)
                load_adj(act, (t + PRELOAD) // WORD, t % WORD, (2, 3))
            with act.Fori(1, GROUPS - PRELOAD // WORD) as m:
                for e in range(WORD):
                    copy_aggregate(WORD * m + e, e)
                    act.wait_ge(mask_made, WORD * m + (e + PRELOAD - STAGE + 1))
                    load_adj(act, m + PRELOAD // WORD, e, (2, 3))
            copies = list(range(T - PRELOAD, T - WORD))
            for t in copies[:2]:
                copy_aggregate(t, t % BANKS)
            for m in range(GROUPS):
                root(m)
                if m >= 1:
                    normalise(m - 1)
                if m + 2 < len(copies):
                    copy_aggregate(copies[m + 2], copies[m + 2] % BANKS)
            normalise(GROUPS - 1)

        @block.vector
        def _(dve):
            nc.vector.memset(eps, EPS).then_inc(zeros_ready, 1)
            nc.vector.memset(ones, 1.0).then_inc(zeros_ready, 1)
            nc.vector.memset(deg_acc[:], 0).then_inc(zeros_ready, 1)
            dve.wait_ge(w_landed, 32)

            def mask_bytes(t, r, turn, first):
                dve.wait_ge(adj_landed[r % STAGE], 16 * QUADS * (turn + 1))
                if not (first and r == 0):
                    dve.wait_ge(maskT_ready, t)
                nc.vector.tensor_scalar(mask8[:], adj_f[:, r % STAGE], 0.0, float(MARK), ALU.not_equal,
                                        ALU.mult).then_inc(mask_made, 1)

            def turn_mask(t, r, first):
                dve.wait_ge(mask_made, t + 1)
                if not first:
                    dve.wait_ge(agg_full, t - (RING - 1))
                nc.vector.transpose(
                    maskT[:, r].rearrange("p m (g a) -> p g m a", g=QUADS),
                    mask8[:].bitcast(U32).rearrange("p g (m a) -> p g m a", m=GROUPS)).then_inc(maskT_ready, 1)

            def count_edges(t, r, first):
                dve.wait_ge(maskT_ready, t + 1)
                if first and r == 0:
                    dve.wait_ge(zeros_ready, 3)
                else:
                    dve.wait_ge(deg_added, t)
                nc.vector.tensor_tensor(deg_acc[:].bitcast(U16), deg_acc[:].bitcast(U16),
                                        maskT[:, r].bitcast(U16), ALU.add).then_inc(deg_added, 1)

            def mask_slab(t, r, turn, first):
                mask_bytes(t, r, turn, first)
                turn_mask(t, r, first)
                count_edges(t, r, first)

            def hidden_pair(u):
                dve.wait_ge(h_ready, u + 1)
                nc.vector.tensor_tensor(g_sb[:, 2 * u:2 * u + 2, :], h_ps[:, u % 2],
                                        b_sb.rearrange("p (k f) -> p k f", k=1).broadcast_to([P, 2, F]),
                                        ALU.add).then_inc(h_biased, 1)

            def max_x(m):
                dve.wait_ge(x_landed[x_chunk_of(m)], 16 * QUADS)
                nc.vector.tensor_reduce(x_max[:, m:m + 1], x_sb[:, WORD * m:WORD * (m + 1), :], AX.XY, ALU.max,
                                        apply_absolute_value=True).then_inc(x_maxed, 1)

            def split_lo(u):
                dve.wait_ge(hi_ready, u + 1)
                nc.vector.scalar_tensor_tensor(out=parts[:, 2 * u:2 * u + 2, F:2 * F], in0=g_sb[:, 2 * u:2 * u + 2, :],
                                               scalar=scale, in1=parts[:, 2 * u:2 * u + 2, 0:F], op0=ALU.mult,
                                               op1=ALU.subtract).then_inc(lo_ready, 1)

            nc.vector.tensor_reduce(part_max[:, 1:2], w_sb, AX.XY, ALU.max,
                                    apply_absolute_value=True).then_inc(max_step, 1)
            nc.vector.tensor_reduce(b_max, b_sb, AX.X, ALU.max, apply_absolute_value=True).then_inc(max_step, 1)
            for u in range(PAIRS):
                hidden_pair(u)
                if u < GROUPS:
                    max_x(u)
                if u == TURN - 1:
                    dve.wait_ge(x_maxed, GROUPS)
                    nc.vector.tensor_reduce(part_max[:, 0:1], x_max[:], AX.X, ALU.max).then_inc(max_step, 1)
                if u == TURN:
                    dve.wait_ge(max_turned, 1)
                    nc.vector.tensor_reduce(all_max[0:1], max_rows, AX.X, ALU.max).then_inc(max_step, 1)
                if u == SPREAD:
                    dve.wait_ge(max_spread, 1)
                    nc.vector.tensor_copy(both_max, max_cols).then_inc(max_step, 1)
                    dve.wait_ge(max_step, 5)
                    nc.vector.tensor_tensor(lead, both_max[:, 0:1], both_max[:, 1:2], ALU.mult).then_inc(max_step, 1)
                    dve.wait_ge(max_step, 6)
                    nc.vector.scalar_tensor_tensor(out=unscale, in0=lead, scalar=float(F), in1=b_max, op0=ALU.mult,
                                                   op1=ALU.add).then_inc(max_step, 1)
                    dve.wait_ge(max_step, 7)
                    nc.vector.tensor_scalar(lead, unscale, 2.0 ** -100, 2.0 ** 120, ALU.max, ALU.min).then_inc(max_step, 1)
                    dve.wait_ge(max_step, 8)
                    nc.vector.tensor_scalar(unscale.bitcast(U32), lead.bitcast(U32), 0x7F800000, None,
                                            ALU.bitwise_and).then_inc(max_step, 1)
                    dve.wait_ge(max_step, 9)
                    nc.vector.reciprocal(lead, unscale).then_inc(max_step, 1)
                    dve.wait_ge(max_step, 10)
                    nc.vector.tensor_scalar(scale, lead, 2.0 ** 14, None, ALU.mult).then_inc(scale_ready, 1)
                    dve.wait_ge(scale_ready, 1)
                for k in split_after[u]:
                    split_lo(k)
            mask_bytes(0, 0, 0, True)
            turn_mask(0, 0, True)
            for k in split_after[PAIRS]:
                split_lo(k)
            count_edges(0, 0, True)
            for r in range(1, RING):
                mask_slab(r, r, r // STAGE, True)
            with dve.Fori(1, T // RING) as i:
                for r in range(RING):
                    mask_slab(RING * i + r, r, (RING // STAGE) * i + r // STAGE, False)

            dve.wait_ge(deg_added, T)
            deg_bytes = deg_acc[:].bitcast(U8).rearrange("p m (i e) -> p m e i", e=WORD)
            nc.vector.tensor_reduce(deg4[:].rearrange("p (m e) -> p m e", e=WORD), deg_bytes,
                                    AX.X, ALU.add).then_inc(deg_step, 1)
            dve.wait_ge(deg_step, 1)
            nc.vector.reciprocal(rdeg4[:], deg4[:]).then_inc(deg_step, 1)
            dve.wait_ge(deg_step, 2)
            nc.vector.tensor_scalar(inv_deg[:], rdeg4[:], unscale, float(MARK), ALU.mult, ALU.mult).then_inc(deg_step, 1)
            dve.wait_ge(deg_step, 3)

            def row_stats(m, k, last=False):
                for e in range(WORD):
                    t = WORD * m + e
                    y, factor = g_sb[:, bass.ds(t, 1), :], inv_deg[:, bass.ds(t, 1)]
                    if last:
                        dve.wait_ge(agg_full, t + 1)
                        nc.vector.scalar_tensor_tensor(out=g_sb[:, t, :], in0=agg[:, e, 0:F], scalar=factor,
                                                       in1=x_sb[:, t, :], op0=ALU.mult,
                                                       op1=ALU.add).then_inc(hi_added, 1)
                        dve.wait_ge(hi_added, e + 1)
                        nc.vector.scalar_tensor_tensor(out=g_sb[:, t, :], in0=agg[:, e, F:2 * F], scalar=factor,
                                                       in1=g_sb[:, t, :], op0=ALU.mult,
                                                       op1=ALU.add).then_inc(y_ready, 1)
                    else:
                        dve.wait_ge(g_ready, t + 1)
                        nc.vector.scalar_tensor_tensor(out=y, in0=y, scalar=factor, in1=x_sb[:, bass.ds(t, 1), :],
                                                       op0=ALU.mult, op1=ALU.add).then_inc(y_ready, 1)
                for e in range(WORD):
                    t = WORD * m + e
                    dve.wait_ge(deg_step, 3)
                    dve.wait_ge(y_ready, t + 1)
                    nc.vector.bn_stats(stats[:, e, :], g_sb[:, bass.ds(t, 1), :]).then_inc(stats_ready, 1)
                for e in range(WORD):
                    dve.wait_ge(deg_step, 3)
                    dve.wait_ge(stats_ready, WORD * m + (e + 1))
                    nc.vector.bn_aggr(mv[:, k, e, :], stats[:, e, :]).then_inc(mv_ready, 1)

            def row_factors(m, k):
                var, inv, t = mv[:, k, :, 1], rstd[:, k], newton[:, k]
                dve.wait_ge(std_ready, m + 1)
                nc.vector.reciprocal(std[:, k], std[:, k]).then_inc(newton_step, 1)
                dve.wait_ge(newton_step, 4 * m + 1)
                nc.vector.scalar_tensor_tensor(out=t, in0=var, scalar=EPS, in1=std[:, k], op0=ALU.add,
                                               op1=ALU.mult).then_inc(newton_step, 1)
                dve.wait_ge(newton_step, 4 * m + 2)
                nc.vector.scalar_tensor_tensor(out=inv, in0=t, scalar=-0.5, in1=std[:, k], op0=ALU.mult,
                                               op1=ALU.mult).then_inc(newton_step, 1)
                dve.wait_ge(newton_step, 4 * m + 3)
                nc.vector.scalar_tensor_tensor(out=inv, in0=inv, scalar=1.5, in1=std[:, k], op0=ALU.add,
                                               op1=ALU.mult).then_inc(newton_step, 1)
                dve.wait_ge(newton_step, 4 * m + 4)
                nc.vector.scalar_tensor_tensor(out=shift[:, k], in0=mv[:, k, :, 0], scalar=-1.0, in1=inv,
                                               op0=ALU.mult, op1=ALU.mult).then_inc(shift_ready, 1)

            row_stats(0, 0)
            row_stats(1, 1)
            row_factors(0, 0)
            with dve.Fori(1, GROUPS // 2 - 1) as i:
                for k in range(2):
                    dve.wait_ge(std_ready, 2 * i + (k - 1))
                    row_stats(2 * i + k, k)
                    dve.wait_ge(out_ready, WORD * (2 * i + (k - 2)))
                    row_factors(2 * i + (k - 1), 1 - k)
            for m in (GROUPS - 2, GROUPS - 1):
                dve.wait_ge(std_ready, m - 1)
                row_stats(m, m % 2, m == GROUPS - 1)
                dve.wait_ge(out_ready, WORD * (m - 2))
                row_factors(m - 1, 1 - m % 2)
            dve.wait_ge(out_ready, WORD * (GROUPS - 2))
            row_factors(GROUPS - 1, 1)

        @block.tensor
        def _(pe):
            pe.wait_ge(ident_ready, 1)
            pe.wait_ge(w_landed, 32)
            for u in range(PAIRS + 1):
                if u < PAIRS:
                    if 2 * u % WORD == 0 and 2 * u // WORD in X_FROM:
                        pe.wait_ge(x_landed[X_FROM.index(2 * u // WORD)], 16 * QUADS)
                    if u >= 2:
                        pe.wait_ge(xT_copied, u - 1)
                    for j in range(2 * KC):
                        last = nc.tensor.transpose(xT_ps[:, u % 2, j, :], x_sb[:, 2 * u + j // KC, (j % KC) * P:(j % KC + 1) * P], ident)
                    last.then_inc(xT_ready, 1)
                if u >= 1:
                    v = u - 1
                    pe.wait_ge(xT_copied, v + 1)
                    if v >= 2:
                        pe.wait_ge(h_biased, v - 1)
                    for k in range(2):
                        for c in range(KC):
                            last = nc.tensor.matmul(h_ps[:, v % 2, k, :], xT_sb[:, v % 2, KC * k + c, :], w_sb[:, c, :],
                                                    start=(c == 0), stop=(c == KC - 1))
                    last.then_inc(h_ready, 1)
                if u == TURN + 1:
                    pe.wait_ge(max_step, 3)
                    for k in range(2):
                        last = nc.tensor.transpose(max_rows[:, k, :], part_max[:, k:k + 1], ident)
                    last.then_inc(max_turned, 1)
                if u == SPREAD + 1:
                    pe.wait_ge(zeros_ready, 3)
                    pe.wait_ge(max_step, 4)
                    nc.tensor.matmul(max_cols, ones[0:1, :], all_max[0:1, :], start=True,
                                     stop=True).then_inc(max_spread, 1)

            def aggregate(t, r, first):
                if not first:
                    pe.reg_add(slabs_turned, slabs_turned, 1)
                    pe.reg_add(slabs_copied, slabs_copied, 1)
                    pe.wait_ge(lo_ready, PAIRS)
                    pe.wait_ge(maskT_ready, slabs_turned)
                    pe.wait_ge(agg_copied, slabs_copied)
                else:
                    pe.wait_ge(maskT_ready, t + 1)
                    if r >= BANKS:
                        pe.wait_ge(agg_copied, t - (BANKS - 1))
                for k in range(T):
                    if first and r == 0 and k % 2 == 0:
                        pe.wait_ge(lo_ready, k // 2 + 1)
                    words = maskT[:, r, k // WORD, :].bitcast(F8)
                    last = nc.tensor.matmul(agg[:, r % BANKS, :], words[:, k % WORD::WORD], parts[:, k, :],
                                            start=(k == 0), stop=(k == T - 1))
                last.then_inc(agg_full, 1)

            for r in range(RING):
                aggregate(r, r, True)
            slabs_turned, slabs_copied = pe.alloc_register("slabs_turned"), pe.alloc_register("slabs_copied")
            pe.reg_mov(slabs_turned, RING)
            pe.reg_mov(slabs_copied, RING - BANKS)
            with pe.Fori(1, T // RING) as i:
                for r in range(RING):
                    aggregate(RING * i + r, r, False)


_INS = ["x", "adj", "L0_gnn_W", "L0_gnn_b"]
_OUTS = [((4096, 256), "float32")]


def kernel(**inputs):
    import numpy as _np
    import concourse.bacc as _bacc
    from concourse import mybir as _mybir
    from concourse.bass_utils import run_bass_kernel_spmd as _run

    nc = _bacc.Bacc("TRN2", target_bir_lowering=False, num_devices=1)
    arrays, args = {}, []
    for name in _INS:
        a = _np.ascontiguousarray(inputs[name])
        arrays[f"in_{name}_dram"] = a
        args.append(nc.dram_tensor(f"in_{name}_dram", a.shape, _mybir.dt.from_np(a.dtype), kind="ExternalInput").ap())
    for i, (shape, dtype) in enumerate(_OUTS):
        dt = _mybir.dt.from_np(_np.dtype(dtype))
        args.append(nc.dram_tensor(f"out_{i}_dram", shape, dt, kind="ExternalOutput").ap())
    build(nc, *args)
    r = _run(nc, [arrays], core_ids=[0])
    got = tuple(r.results[0][f"out_{i}_dram"] for i in range(len(_OUTS)))
    return got[0]
```

```python
from contextlib import ExitStack

import concourse.bass as bass
from concourse import mybir

P = 128
QUADS = 4
QP = P // QUADS
WORD = 4
MARK = 4
STAGE = 4
RING = 8
BANKS = 4
X_CHUNKS = (1, 3, 4)
TURN, SPREAD, SPLIT = 7, 8, 9
MASK_AT, TURN_AT = 7, 8
LOAD_AT = (1, 3, 5, 7)
EPS = 1e-5
WARM_UP = 8

F32, F16, F8 = mybir.dt.float32, mybir.dt.float16, mybir.dt.float8e5
U8, U16, U32 = mybir.dt.uint8, mybir.dt.uint16, mybir.dt.uint32
ALU, ACT, AX = mybir.AluOpType, mybir.ActivationFunctionType, mybir.AxisListType


def build(nc, x, adj, w, b, out):
    N, F = x.shape
    T = N // P
    GROUPS = T // WORD
    QC = N // QUADS
    KC = F // P
    PAIRS = T // 2
    X_FROM = [sum(X_CHUNKS[:c]) for c in range(len(X_CHUNKS) + 1)]
    PRELOAD = RING
    assert T % RING == 0 and RING % STAGE == 0 and RING % BANKS == 0 and F == 256 and T * MARK < 256
    assert QC == GROUPS * QP * WORD and STAGE == WORD

    split_after, k = [[] for _ in range(PAIRS + 1)], 0
    for u in range(SPLIT, PAIRS):
        while k <= u - 1 and len(split_after[u]) < 2:
            split_after[u].append(k)
            k += 1
    split_after[PAIRS] = list(range(k, PAIRS))

    x_v = x.rearrange("(q m a e) f -> q a m (e f)", q=QUADS, m=GROUPS, a=QP, e=WORD)
    out_v = out.rearrange("(q m a e) f -> m q a (e f)", q=QUADS, m=GROUPS, a=QP, e=WORD)
    adj_v = adj.rearrange("(r m a e) (q c) -> m e q a r c", r=QUADS, m=GROUPS, a=QP, e=WORD, q=QUADS)
    w_v = w.rearrange("(c p) f -> p c f", c=KC)

    with ExitStack() as ctx:
        def sb(name, shape, dt):
            return ctx.enter_context(nc.sbuf_tensor(name, shape, dt))

        def sem(name):
            return ctx.enter_context(nc.semaphore(name))

        agg = ctx.enter_context(nc.psum_tensor("agg", [P, BANKS, 2 * F], F32))
        xT_ps = ctx.enter_context(nc.psum_tensor("xT_ps", [P, 2, 2 * KC, P], F32))
        h_ps = ctx.enter_context(nc.psum_tensor("h_ps", [P, 2, 2, F], F32))

        x_sb = sb("x_sb", [P, T, F], F32)
        g_sb = sb("g_sb", [P, T, F], F32)
        parts = sb("parts", [P, T, 2 * F], F16)
        adj_f = sb("adj_f", [P, STAGE, QUADS, QC], F32)
        mask8 = sb("mask8", [P, QUADS, QC], U8)
        maskT = sb("maskT", [P, RING, GROUPS, P], U32)
        hilo = sb("hilo", [P, 2, 2 * F], F32)
        deg_acc = sb("deg_acc", [P, GROUPS, P], U32)
        stats = sb("stats", [P, WORD, 6], F32)
        mv = sb("mv", [P, 2, WORD, 2], F32)
        std = sb("std", [P, 2, WORD], F32)
        rstd = sb("rstd", [P, 2, WORD], F32)
        shift = sb("shift", [P, 2, WORD], F32)
        rdeg4 = sb("rdeg4", [P, T], F32)
        newton = sb("newton", [P, 2, WORD], F32)
        deg4 = sb("deg4", [P, T], F32)
        inv_deg = sb("inv_deg", [P, T], F32)
        x_max = sb("x_max", [P, GROUPS], F32)
        col = sb("col", [P, 12], F32)
        early = maskT[:, RING - 2:RING].rearrange("p r m n -> p (r m n)").bitcast(F32)
        w_sb = early[:, 0:KC * F].rearrange("p (c f) -> p c f", c=KC)
        b_sb = early[:, 512:512 + F]
        ident = early[:, 768:768 + P]
        ones = early[:, 896:896 + P]
        xT_sb = early[:, 1024:2048].rearrange("p (k j n) -> p k j n", k=2, j=2 * KC)
        part_max, all_max, both_max = col[:, 0:2], col[:, 2:4], col[:, 4:6]
        b_max, lead, scale, unscale, eps, warm = (col[:, i:i + 1] for i in range(6, 12))
        max_rows, max_cols = agg[0:1, 2, 0:2 * P].rearrange("p (k n) -> p k n", k=2), agg[:, 3, 0:2]

        w_landed = sem("w_landed")
        x_landed = [sem(f"x_landed{c}") for c in range(len(X_CHUNKS))]
        adj_landed = [sem(f"adj_landed{s}") for s in range(STAGE)]
        ident_zero, ident_ready = sem("ident_zero"), sem("ident_ready")
        zeros_ready = sem("zeros_ready")
        xT_ready, xT_copied = sem("xT_ready"), sem("xT_copied")
        h_ready, h_biased, x_maxed = sem("h_ready"), sem("h_biased"), sem("x_maxed")
        max_step, max_turned, max_spread = sem("max_step"), sem("max_turned"), sem("max_spread")
        scale_ready = sem("scale_ready")
        hi_ready, lo_ready = sem("hi_ready"), sem("lo_ready")
        mask_made, maskT_ready, deg_added = sem("mask_made"), sem("maskT_ready"), sem("deg_added")
        agg_full, agg_copied, g_ready = sem("agg_full"), sem("agg_copied"), sem("g_ready")
        deg_step = sem("deg_step")
        hi_added = sem("hi_added")
        y_ready, stats_ready, mv_ready = sem("y_ready"), sem("stats_ready"), sem("mv_ready")
        std_ready, newton_step, shift_ready = sem("std_ready"), sem("newton_step"), sem("shift_ready")
        out_ready, out_stored = sem("out_ready"), sem("out_stored")

        def load_adj(queue, m, e, quads):
            for q in quads:
                queue.dma_start(adj_f[q * QP:(q + 1) * QP, e], adj_v[m, e, q]).then_inc(adj_landed[e], 16)

        def load_x(queue, c, quads):
            for q in quads:
                queue.dma_start(x_sb[q * QP:(q + 1) * QP, X_FROM[c] * WORD:X_FROM[c + 1] * WORD, :],
                                x_v[q, :, X_FROM[c]:X_FROM[c + 1]]).then_inc(x_landed[c], 16)

        def store_last(queue, quads, tiles):
            m, fs = GROUPS - 1, slice(tiles.start * F, tiles.stop * F)
            for q in quads:
                queue.dma_start(out_v[m, q, :, fs],
                                g_sb[q * QP:(q + 1) * QP, WORD * m + tiles.start:WORD * m + tiles.stop, :]
                                ).then_inc(out_stored, 16)

        def x_chunk_of(group):
            return max(c for c in range(len(X_CHUNKS)) if X_FROM[c] <= group)

        block = ctx.enter_context(nc.Block())

        @block.sync
        def _(sp):
            load_x(sp, 0, (0,))
            sp.dma_start(w_sb, w_v).then_inc(w_landed, 16)
            load_x(sp, 0, (1,))
            for c in range(1, len(X_CHUNKS)):
                load_x(sp, c, (0, 1))
            for e in range(STAGE):
                load_adj(sp, 0, e, (0, 1))
            with sp.Fori(1, GROUPS) as m:
                for e in range(WORD):
                    sp.wait_ge(mask_made, WORD * m + (e - STAGE + 1))
                    load_adj(sp, m, e, (0, 1))
            with sp.Fori(0, GROUPS - 1) as m:
                sp.wait_ge(out_ready, WORD * m + WORD)
                for q in range(QUADS):
                    sp.dma_start(out_v[m, q],
                                 g_sb[q * QP:(q + 1) * QP, bass.ts(m, WORD), :]).then_inc(out_stored, 16)
            sp.wait_ge(out_ready, T - 1)
            store_last(sp, range(QUADS), slice(0, WORD - 1))
            sp.wait_ge(out_ready, T)
            store_last(sp, (0, 1), slice(WORD - 1, WORD))
            sp.wait_ge(out_stored, 16 * QUADS * (GROUPS + 1))

        @block.gpsimd
        def _(pool):
            nc.gpsimd.memset(ident, 0.0).then_inc(ident_zero, 1)
            pool.wait_ge(ident_zero, 1)
            nc.gpsimd.affine_select(out=ident, in_=ident, compare_op=ALU.not_equal, fill=1.0, base=0,
                                    pattern=[[-1, P]], channel_multiplier=1).then_inc(ident_ready, 1)
            with pool.Fori(0, (T - WORD) // 2) as i:
                for j in range(2):
                    pool.wait_ge(agg_copied, 2 * i + (j + 1))
                    nc.gpsimd.tensor_tensor(g_sb[:, bass.ds(2 * i + j, 1), :], hilo[:, j:j + 1, 0:F],
                                            hilo[:, j:j + 1, F:2 * F], ALU.add).then_inc(g_ready, 1)

        @block.scalar
        def _(act):
            load_x(act, 0, (2, 3))
            act.dma_start(b_sb, b.rearrange("(a f) -> a f", a=1).broadcast_to([P, F])).then_inc(w_landed, 16)
            load_x(act, 1, (2, 3))
            act.wait_ge(zeros_ready, 1)
            nc.scalar.copy(warm, eps)

            def split_hi(u):
                act.wait_ge(h_biased, u + 1)
                nc.scalar.activation(parts[:, 2 * u:2 * u + 2, 0:F], g_sb[:, 2 * u:2 * u + 2, :],
                                     ACT.Copy, scale=scale).then_inc(hi_ready, 1)

            for u in range(PAIRS):
                act.wait_ge(xT_ready, u + 1)
                if u >= 2:
                    act.wait_ge(h_ready, u - 1)
                nc.scalar.copy(xT_sb[:, u % 2], xT_ps[:, u % 2]).then_inc(xT_copied, 1)
                if u + 2 < len(X_CHUNKS):
                    load_x(act, u + 2, (2, 3))
                if u in LOAD_AT:
                    load_adj(act, 0, LOAD_AT.index(u), (2, 3))
                if u == SPLIT + 1:
                    act.wait_ge(scale_ready, 1)
                for k in split_after[max(u - 1, 0)]:
                    split_hi(k)
            for k in split_after[PAIRS - 1] + split_after[PAIRS]:
                split_hi(k)
            for t in range(STAGE, PRELOAD):
                act.wait_ge(mask_made, t - STAGE + 1)
                load_adj(act, t // WORD, t % WORD, (2, 3))

            def copy_aggregate(t, k):
                act.wait_ge(agg_full, t + 1)
                act.wait_ge(g_ready, t - 1)
                nc.scalar.copy(hilo[:, k % 2], agg[:, k]).then_inc(agg_copied, 1)

            def normalise(m):
                act.wait_ge(shift_ready, m + 1)
                for e in range(WORD if m < GROUPS - 1 else WORD - 1):
                    nc.scalar.activation(g_sb[:, WORD * m + e, :], g_sb[:, WORD * m + e, :], ACT.Identity,
                                         scale=rstd[:, m % 2, e:e + 1],
                                         bias=shift[:, m % 2, e:e + 1]).then_inc(out_ready, 1)

            def root(m, tiles=slice(0, WORD)):
                act.wait_ge(mv_ready, WORD * m + tiles.stop)
                nc.scalar.activation(std[:, m % 2, tiles], mv[:, m % 2, tiles, 1], ACT.Sqrt,
                                     bias=eps).then_inc(std_ready, 1)

            for t in range(BANKS):
                act.wait_ge(agg_full, t + 1)
                if t >= 2:
                    act.wait_ge(g_ready, t - 1)
                nc.scalar.copy(hilo[:, t % 2], agg[:, t]).then_inc(agg_copied, 1)
                act.wait_ge(mask_made, t + PRELOAD - STAGE + 1)
                load_adj(act, (t + PRELOAD) // WORD, t % WORD, (2, 3))
            with act.Fori(1, GROUPS - PRELOAD // WORD) as m:
                for e in range(WORD):
                    copy_aggregate(WORD * m + e, e)
                    act.wait_ge(mask_made, WORD * m + (e + PRELOAD - STAGE + 1))
                    load_adj(act, m + PRELOAD // WORD, e, (2, 3))
            copies = list(range(T - PRELOAD, T - WORD))
            for t in copies[:2]:
                copy_aggregate(t, t % BANKS)
            for m in range(GROUPS - 1):
                root(m)
                if m >= 1:
                    normalise(m - 1)
                if m + 2 < len(copies):
                    copy_aggregate(copies[m + 2], copies[m + 2] % BANKS)
            normalise(GROUPS - 2)
            root(GROUPS - 1, slice(0, WORD - 1))
            normalise(GROUPS - 1)
            root(GROUPS - 1, slice(WORD - 1, WORD))
            act.wait_ge(out_ready, T)
            store_last(act, (2, 3), slice(WORD - 1, WORD))

        @block.vector
        def _(dve):
            nc.vector.memset(eps, EPS).then_inc(zeros_ready, 1)
            nc.vector.memset(ones, 1.0).then_inc(zeros_ready, 1)
            nc.vector.memset(deg_acc[:], 0).then_inc(zeros_ready, 1)
            dve.wait_ge(w_landed, 32)

            def mask_bytes(t, r, turn, first):
                dve.wait_ge(adj_landed[r % STAGE], 16 * QUADS * (turn + 1))
                if not (first and r == 0):
                    dve.wait_ge(maskT_ready, t)
                nc.vector.tensor_scalar(mask8[:], adj_f[:, r % STAGE], 0.0, float(MARK), ALU.not_equal,
                                        ALU.mult).then_inc(mask_made, 1)

            def turn_mask(t, r, first):
                dve.wait_ge(mask_made, t + 1)
                if not first:
                    dve.wait_ge(agg_full, t - (RING - 1))
                nc.vector.transpose(
                    maskT[:, r].rearrange("p m (g a) -> p g m a", g=QUADS),
                    mask8[:].bitcast(U32).rearrange("p g (m a) -> p g m a", m=GROUPS)).then_inc(maskT_ready, 1)

            def count_edges(t, r, first):
                dve.wait_ge(maskT_ready, t + 1)
                if first and r == 0:
                    dve.wait_ge(zeros_ready, 3)
                else:
                    dve.wait_ge(deg_added, t)
                nc.vector.tensor_tensor(deg_acc[:].bitcast(U16), deg_acc[:].bitcast(U16),
                                        maskT[:, r].bitcast(U16), ALU.add).then_inc(deg_added, 1)

            def mask_slab(t, r, turn, first):
                mask_bytes(t, r, turn, first)
                turn_mask(t, r, first)
                count_edges(t, r, first)

            def hidden_pair(u):
                dve.wait_ge(h_ready, u + 1)
                nc.vector.tensor_tensor(g_sb[:, 2 * u:2 * u + 2, :], h_ps[:, u % 2],
                                        b_sb.rearrange("p (k f) -> p k f", k=1).broadcast_to([P, 2, F]),
                                        ALU.add).then_inc(h_biased, 1)

            def max_x(m):
                dve.wait_ge(x_landed[x_chunk_of(m)], 16 * QUADS)
                nc.vector.tensor_reduce(x_max[:, m:m + 1], x_sb[:, WORD * m:WORD * (m + 1), :], AX.XY, ALU.max,
                                        apply_absolute_value=True).then_inc(x_maxed, 1)

            def split_lo(u):
                dve.wait_ge(hi_ready, u + 1)
                nc.vector.scalar_tensor_tensor(out=parts[:, 2 * u:2 * u + 2, F:2 * F], in0=g_sb[:, 2 * u:2 * u + 2, :],
                                               scalar=scale, in1=parts[:, 2 * u:2 * u + 2, 0:F], op0=ALU.mult,
                                               op1=ALU.subtract).then_inc(lo_ready, 1)

            nc.vector.tensor_reduce(part_max[:, 1:2], w_sb, AX.XY, ALU.max,
                                    apply_absolute_value=True).then_inc(max_step, 1)
            nc.vector.tensor_reduce(b_max, b_sb, AX.X, ALU.max, apply_absolute_value=True).then_inc(max_step, 1)
            max_x(0)
            for u in range(PAIRS):
                hidden_pair(u)
                if u < GROUPS - 1:
                    max_x(u + 1)
                if u == TURN - 1:
                    dve.wait_ge(x_maxed, GROUPS)
                    nc.vector.tensor_reduce(part_max[:, 0:1], x_max[:], AX.X, ALU.max).then_inc(max_step, 1)
                if u == TURN:
                    dve.wait_ge(max_turned, 1)
                    nc.vector.tensor_reduce(all_max[0:1], max_rows, AX.X, ALU.max).then_inc(max_step, 1)
                if u == SPREAD:
                    dve.wait_ge(max_spread, 1)
                    nc.vector.tensor_copy(both_max, max_cols).then_inc(max_step, 1)
                    dve.wait_ge(max_step, 5)
                    nc.vector.tensor_tensor(lead, both_max[:, 0:1], both_max[:, 1:2], ALU.mult).then_inc(max_step, 1)
                    dve.wait_ge(max_step, 6)
                    nc.vector.scalar_tensor_tensor(out=unscale, in0=lead, scalar=float(F), in1=b_max, op0=ALU.mult,
                                                   op1=ALU.add).then_inc(max_step, 1)
                    dve.wait_ge(max_step, 7)
                    nc.vector.tensor_scalar(lead, unscale, 2.0 ** -100, 2.0 ** 120, ALU.max, ALU.min).then_inc(max_step, 1)
                    dve.wait_ge(max_step, 8)
                    nc.vector.tensor_scalar(unscale.bitcast(U32), lead.bitcast(U32), 0x7F800000, None,
                                            ALU.bitwise_and).then_inc(max_step, 1)
                    dve.wait_ge(max_step, 9)
                    nc.vector.reciprocal(lead, unscale).then_inc(max_step, 1)
                    dve.wait_ge(max_step, 10)
                    nc.vector.tensor_scalar(scale, lead, 2.0 ** 14, None, ALU.mult).then_inc(scale_ready, 1)
                    dve.wait_ge(scale_ready, 1)
                for k in split_after[u]:
                    split_lo(k)
                if u == MASK_AT:
                    mask_bytes(0, 0, 0, True)
                if u == TURN_AT:
                    turn_mask(0, 0, True)
            for k in split_after[PAIRS]:
                split_lo(k)
            mask_bytes(1, 1, 0, True)
            turn_mask(1, 1, True)
            count_edges(0, 0, True)
            count_edges(1, 1, True)
            for r in range(2, RING):
                mask_slab(r, r, r // STAGE, True)
            with dve.Fori(1, T // RING) as i:
                for r in range(RING):
                    mask_slab(RING * i + r, r, (RING // STAGE) * i + r // STAGE, False)

            dve.wait_ge(deg_added, T)
            deg_bytes = deg_acc[:].bitcast(U8).rearrange("p m (i e) -> p m e i", e=WORD)
            nc.vector.tensor_reduce(deg4[:].rearrange("p (m e) -> p m e", e=WORD), deg_bytes,
                                    AX.X, ALU.add).then_inc(deg_step, 1)
            dve.wait_ge(deg_step, 1)
            nc.vector.reciprocal(rdeg4[:], deg4[:]).then_inc(deg_step, 1)
            dve.wait_ge(deg_step, 2)
            nc.vector.tensor_scalar(inv_deg[:], rdeg4[:], unscale, float(MARK), ALU.mult, ALU.mult).then_inc(deg_step, 1)
            dve.wait_ge(deg_step, 3)

            def moments(m, k, tiles):
                for e in tiles:
                    dve.wait_ge(deg_step, 3)
                    dve.wait_ge(y_ready, WORD * m + (e + 1))
                    nc.vector.bn_stats(stats[:, e, :], g_sb[:, bass.ds(WORD * m + e, 1), :]).then_inc(stats_ready, 1)
                for e in tiles:
                    dve.wait_ge(deg_step, 3)
                    dve.wait_ge(stats_ready, WORD * m + (e + 1))
                    nc.vector.bn_aggr(mv[:, k, e, :], stats[:, e, :]).then_inc(mv_ready, 1)

            def row_stats(m, k):
                for e in range(WORD):
                    t = WORD * m + e
                    y = g_sb[:, bass.ds(t, 1), :]
                    dve.wait_ge(g_ready, t + 1)
                    nc.vector.scalar_tensor_tensor(out=y, in0=y, scalar=inv_deg[:, bass.ds(t, 1)],
                                                   in1=x_sb[:, bass.ds(t, 1), :], op0=ALU.mult,
                                                   op1=ALU.add).then_inc(y_ready, 1)
                moments(m, k, range(WORD))

            def row_stats_last(tiles):
                m = GROUPS - 1
                for e in tiles:
                    t = WORD * m + e
                    y, factor = g_sb[:, t, :], inv_deg[:, t:t + 1]
                    dve.wait_ge(agg_full, t + 1)
                    nc.vector.scalar_tensor_tensor(out=y, in0=agg[:, e, 0:F], scalar=factor, in1=x_sb[:, t, :],
                                                   op0=ALU.mult, op1=ALU.add).then_inc(hi_added, 1)
                    dve.wait_ge(hi_added, e + 1)
                    nc.vector.scalar_tensor_tensor(out=y, in0=agg[:, e, F:2 * F], scalar=factor, in1=y,
                                                   op0=ALU.mult, op1=ALU.add).then_inc(y_ready, 1)
                moments(m, m % 2, tiles)

            def row_factors(n, k, tiles=slice(0, WORD)):
                mean, var = mv[:, k, tiles, 0], mv[:, k, tiles, 1]
                rough, inv, t = std[:, k, tiles], rstd[:, k, tiles], newton[:, k, tiles]
                dve.wait_ge(std_ready, n + 1)
                nc.vector.reciprocal(rough, rough).then_inc(newton_step, 1)
                dve.wait_ge(newton_step, 4 * n + 1)
                nc.vector.scalar_tensor_tensor(out=t, in0=var, scalar=EPS, in1=rough, op0=ALU.add,
                                               op1=ALU.mult).then_inc(newton_step, 1)
                dve.wait_ge(newton_step, 4 * n + 2)
                nc.vector.scalar_tensor_tensor(out=inv, in0=t, scalar=-0.5, in1=rough, op0=ALU.mult,
                                               op1=ALU.mult).then_inc(newton_step, 1)
                dve.wait_ge(newton_step, 4 * n + 3)
                nc.vector.scalar_tensor_tensor(out=inv, in0=inv, scalar=1.5, in1=rough, op0=ALU.add,
                                               op1=ALU.mult).then_inc(newton_step, 1)
                if tiles.start:
                    return
                dve.wait_ge(newton_step, 4 * n + 4)
                nc.vector.scalar_tensor_tensor(out=shift[:, k, tiles], in0=mean, scalar=-1.0, in1=inv,
                                               op0=ALU.mult, op1=ALU.mult).then_inc(shift_ready, 1)

            row_stats(0, 0)
            row_stats(1, 1)
            row_factors(0, 0)
            dve.wait_ge(std_ready, 1)
            row_stats(2, 0)
            row_factors(1, 1)
            with dve.Fori(1, GROUPS // 2 - 1) as i:
                for j in range(2):
                    m, k = 2 * i + (1 + j), (1 + j) % 2
                    dve.wait_ge(std_ready, m - 1)
                    row_stats(m, k)
                    dve.wait_ge(out_ready, WORD * (m - 2))
                    row_factors(m - 1, 1 - k)
            m, k = GROUPS - 2, 0
            dve.wait_ge(out_ready, WORD * (m - 1))
            row_factors(m, k)
            dve.wait_ge(std_ready, m)
            row_stats_last(range(0, WORD - 1))
            dve.wait_ge(out_ready, WORD * m)
            row_factors(m + 1, 1 - k, slice(0, WORD - 1))
            row_stats_last(range(WORD - 1, WORD))
            row_factors(m + 2, 1 - k, slice(WORD - 1, WORD))
            dve.wait_ge(out_ready, T - 1)
            dve.wait_ge(newton_step, 4 * (GROUPS + 1))
            y = g_sb[:, T - 1, :]
            nc.vector.tensor_scalar(y, y, mv[:, 1 - k, WORD - 1, 0:1], rstd[:, 1 - k, WORD - 1:WORD], ALU.subtract,
                                    ALU.mult).then_inc(out_ready, 1)

        @block.tensor
        def _(pe):
            pe.wait_ge(ident_ready, 1)
            for _ in range(WARM_UP):
                nc.tensor.matmul(agg[:, 0, 0:P], ident, ident, start=True, stop=True)
            for u in range(PAIRS + 1):
                if u < PAIRS:
                    if 2 * u % WORD == 0 and 2 * u // WORD in X_FROM:
                        pe.wait_ge(x_landed[X_FROM.index(2 * u // WORD)], 16 * QUADS)
                    if u >= 2:
                        pe.wait_ge(xT_copied, u - 1)
                    for j in range(2 * KC):
                        x_part = x_sb[:, 2 * u + j // KC, (j % KC) * P:(j % KC + 1) * P]
                        last = nc.tensor.transpose(xT_ps[:, u % 2, j, :], x_part, ident)
                    last.then_inc(xT_ready, 1)
                if u >= 1:
                    v = u - 1
                    if v == 0:
                        pe.wait_ge(w_landed, 32)
                    pe.wait_ge(xT_copied, v + 1)
                    if v >= 2:
                        pe.wait_ge(h_biased, v - 1)
                    for k in range(2):
                        for c in range(KC):
                            last = nc.tensor.matmul(h_ps[:, v % 2, k, :], xT_sb[:, v % 2, KC * k + c, :],
                                                    w_sb[:, c, :], start=(c == 0), stop=(c == KC - 1))
                    last.then_inc(h_ready, 1)
                if u == TURN + 1:
                    pe.wait_ge(max_step, 3)
                    for k in range(2):
                        last = nc.tensor.transpose(max_rows[:, k, :], part_max[:, k:k + 1], ident)
                    last.then_inc(max_turned, 1)
                if u == SPREAD + 1:
                    pe.wait_ge(zeros_ready, 3)
                    pe.wait_ge(max_step, 4)
                    nc.tensor.matmul(max_cols, ones[0:1, :], all_max[0:1, :], start=True,
                                     stop=True).then_inc(max_spread, 1)

            def aggregate(t, r, first):
                if not first:
                    pe.reg_add(slabs_turned, slabs_turned, 1)
                    pe.reg_add(slabs_copied, slabs_copied, 1)
                    pe.wait_ge(lo_ready, PAIRS)
                    pe.wait_ge(maskT_ready, slabs_turned)
                    pe.wait_ge(agg_copied, slabs_copied)
                else:
                    pe.wait_ge(maskT_ready, t + 1)
                    if r >= BANKS:
                        pe.wait_ge(agg_copied, t - (BANKS - 1))
                for k in range(T):
                    if first and r == 0 and k % 2 == 0:
                        pe.wait_ge(lo_ready, k // 2 + 1)
                    words = maskT[:, r, k // WORD, :].bitcast(F8)
                    last = nc.tensor.matmul(agg[:, r % BANKS, :], words[:, k % WORD::WORD], parts[:, k, :],
                                            start=(k == 0), stop=(k == T - 1))
                last.then_inc(agg_full, 1)

            for r in range(RING):
                aggregate(r, r, True)
            slabs_turned, slabs_copied = pe.alloc_register("slabs_turned"), pe.alloc_register("slabs_copied")
            pe.reg_mov(slabs_turned, RING)
            pe.reg_mov(slabs_copied, RING - BANKS)
            with pe.Fori(1, T // RING) as i:
                for r in range(RING):
                    aggregate(RING * i + r, r, False)


_INS = ["x", "adj", "L0_gnn_W", "L0_gnn_b"]
_OUTS = [((4096, 256), "float32")]


def kernel(**inputs):
    import numpy as _np
    import concourse.bacc as _bacc
    from concourse import mybir as _mybir
    from concourse.bass_utils import run_bass_kernel_spmd as _run

    nc = _bacc.Bacc("TRN2", target_bir_lowering=False, num_devices=1)
    arrays, args = {}, []
    for name in _INS:
        a = _np.ascontiguousarray(inputs[name])
        arrays[f"in_{name}_dram"] = a
        args.append(nc.dram_tensor(f"in_{name}_dram", a.shape, _mybir.dt.from_np(a.dtype), kind="ExternalInput").ap())
    for i, (shape, dtype) in enumerate(_OUTS):
        dt = _mybir.dt.from_np(_np.dtype(dtype))
        args.append(nc.dram_tensor(f"out_{i}_dram", shape, dt, kind="ExternalOutput").ap())
    build(nc, *args)
    r = _run(nc, [arrays], core_ids=[0])
    got = tuple(r.results[0][f"out_{i}_dram"] for i in range(len(_OUTS)))
    return got[0]
```
